# Optimizing a Trainium2 kernel written in Bass

```python
import numpy as np
import jax
import jax.numpy as jnp

def _softmax(x, axis=-1):
    return jax.nn.softmax(x, axis=axis)

def _gelu(x):
    return jax.nn.gelu(x, approximate=True)

def _silu(x):
    return jax.nn.silu(x)

def _sigmoid(x):
    return jax.nn.sigmoid(x)

def _layernorm(x, axis=-1, eps=1e-05):
    m = jnp.mean(x, axis=axis, keepdims=True)
    v = jnp.var(x, axis=axis, keepdims=True)
    return (x - m) / jnp.sqrt(v + eps)

def _scatter_add(tgt, idx, src, axis=0):
    return tgt.at[idx].add(src)

def _segment_sum(src, seg, n):
    return jax.ops.segment_sum(src, seg, n)
kernel_name = 'mk_cond_resid_d2_seqx_r2_7e80f1'

def setup_inputs(seed: int=0):
    np.random.seed(seed)
    _w = jnp.asarray

    def _rec_inputs():
        import jax
        import jax.numpy as jnp
        _rk = jax.random.key(seed)
        x = -7.109e-05 + 0.9999 * jax.random.normal(jax.random.fold_in(_rk, 1), (64, 128, 2048), jnp.float32)
        _lenS = 128 - jax.random.randint(jax.random.fold_in(_rk, 7), (64,), 0, max(1, 128 // 4) + 1, jnp.int32)
        _lenS2 = 128 - jax.random.randint(jax.random.fold_in(_rk, 8), (64,), 0, max(1, 128 // 4) + 1, jnp.int32)
        itok_B_0_15 = jax.random.randint(jax.random.fold_in(_rk, 11), (64,), 0, 16, jnp.int32)
        itok_B_4_50 = jax.random.randint(jax.random.fold_in(_rk, 12), (64,), 4, 51, jnp.int32)
        return (x, itok_B_0_15, itok_B_4_50)
    x, itok_B_0_15, itok_B_4_50 = _rec_inputs()

    def _L0_cond_setup():
        import jax, jax.numpy as jnp
        import numpy as np
        NUM_CONDITIONS = 16
        IN_CH = 128
        OUT_CH = 128
        B = 64
        T = 2048
        key = jax.random.key(seed)
        k_x, k_w, k_c = jax.random.split(key, 3)
        x = jax.random.normal(k_x, (B, IN_CH, T), dtype=jnp.float32)
        bound = float(np.sqrt(6.0 / IN_CH))
        weights = jax.random.uniform(k_w, (NUM_CONDITIONS, IN_CH, OUT_CH), dtype=jnp.float32, minval=-bound, maxval=bound)
        condition = jax.random.randint(k_c, (B,), 0, NUM_CONDITIONS, dtype=jnp.int64)
        return {'x': x, 'weights': weights, 'condition': condition}
    _L0_cond_all = _L0_cond_setup()
    _L0_cond_in = {k: v for k, v in _L0_cond_all.items() if k in ('weights',)}
    del _L0_cond_all

    def _L1_cond_setup():
        import jax, jax.numpy as jnp
        import numpy as np
        RANK = 16
        ALPHA = 16.0
        SCALING = ALPHA / RANK
        key = jax.random.key(seed)
        k1, k2, k3, k4 = jax.random.split(key, 4)
        batch, n_tok, d_in, d_out, n_adapters, rank = (8, 1024, 2048, 2048, 64, RANK)
        x = jax.random.normal(k1, (batch, n_tok, d_in), dtype=jnp.float32)
        A = jax.random.normal(k2, (n_adapters, d_out, rank), dtype=jnp.float32) * 0.02
        B = jax.random.normal(k3, (n_adapters, rank, d_in), dtype=jnp.float32)
        adapter_ids = jax.random.randint(k4, (batch,), 0, n_adapters, dtype=jnp.int32)
        return {'x': x, 'A': A, 'B': B, 'adapter_ids': adapter_ids}
    _L1_cond_all = _L1_cond_setup()
    _L1_cond_in = {k: v for k, v in _L1_cond_all.items() if k in ('A', 'B')}
    del _L1_cond_all
    return {'x': x, 'itok_B_0_15': itok_B_0_15, 'itok_B_4_50': itok_B_4_50, 'L0_cond_weights': _L0_cond_in['weights'], 'L1_cond_A': _L1_cond_in['A'], 'L1_cond_B': _L1_cond_in['B']}

def reference(x, itok_B_0_15, itok_B_4_50, L0_cond_weights, L1_cond_A, L1_cond_B):
    import jax
    import jax.numpy as jnp

    def _L0_cond_ref(x, weights, condition):
        import jax, jax.numpy as jnp
        import numpy as np
        NUM_CONDITIONS = 16
        IN_CH = 128
        OUT_CH = 128
        B = 64
        T = 2048
        W = weights[condition]
        return jnp.einsum('bct,bcd->bdt', x, W)

    def _L1_cond_ref(x, A, B, adapter_ids):
        import jax, jax.numpy as jnp
        import numpy as np
        RANK = 16
        ALPHA = 16.0
        SCALING = ALPHA / RANK
        B_req = B[adapter_ids]
        A_req = A[adapter_ids]
        Bx = jnp.einsum('bni,bri->bnr', x, B_req)
        out = jnp.einsum('bnr,bor->bno', Bx, A_req)
        return out * SCALING
    x = x + _L0_cond_ref(x, L0_cond_weights, itok_B_0_15)
    x = x + _L1_cond_ref(x, L1_cond_A, L1_cond_B, itok_B_4_50)
    return x

_drawn_inputs = setup_inputs


def setup_inputs(seed=0):
    import zlib

    import numpy as np

    out = dict(_drawn_inputs(seed))
    spreads = {}
    factors = {}
    for name, (base, spread) in spreads.items():
        noise = np.random.default_rng([zlib.crc32(name.encode()), seed]).standard_normal(out[name].shape)
        drawn = base * np.exp(spread * noise) if base else spread * noise
        out[name] = jnp.asarray(drawn.astype(out[name].dtype))
    for name, factor in factors.items():
        out[name] = (out[name] * factor).astype(out[name].dtype)
    return out
```

```python
from contextlib import ExitStack

import concourse.bass as bass
from concourse import mybir

F32 = mybir.dt.float32
F32R = mybir.dt.float32r
I32 = mybir.dt.int32
ALU = mybir.AluOpType

P = 128
BATCHES, CHANNELS, TIME = 64, 128, 2048
CONDITIONS = 16
RANK = 16
HL = 2 * RANK
UNIT = 512
UNITS = TIME // UNIT
CHUNKS = UNIT // P
STRIDE = TIME // P
BODY = 4
TURNS = BATCHES // BODY
SLOTS = BODY * UNITS
AHEAD = 2
BEHIND = UNITS
B_FOLD = TIME // 256
A_PARTS = 4
A_CHUNKS = STRIDE // A_PARTS


def live(count):
    return not (isinstance(count, int) and count <= 0)


def cond_lora_residual(nc, x, cond_ids, adapter_ids, weights, lora_a, lora_b, out):
    a_dram = lora_a.rearrange("n (p j) r -> n p (j r)", j=STRIDE)
    b_dram = lora_b.rearrange("n r (h f) -> n (r h) f", h=B_FOLD)

    with ExitStack() as ctx:
        def sbuf(name, shape, dtype=F32):
            return ctx.enter_context(nc.sbuf_tensor(name, shape, dtype))

        def psum(name):
            return ctx.enter_context(nc.psum_tensor(name, [P, UNIT], F32))

        def sem(name):
            return ctx.enter_context(nc.semaphore(name))

        ident = sbuf("ident", [P, P])
        ident_r = sbuf("ident_r", [P, P], F32R)
        halves_sum = sbuf("halves_sum", [P, RANK])
        m_all = sbuf("m_all", [P, CONDITIONS, P])
        ids = sbuf("ids", [1, 2, BATCHES], I32)

        x_in = [sbuf(f"x_in{k}", [P, TIME]) for k in range(BODY)]
        x_out = [sbuf(f"x_out{k}", [P, TIME]) for k in range(BODY)]
        a_raw = [sbuf(f"a_raw{k}", [P, STRIDE, RANK]) for k in range(BODY)]
        b_raw = [sbuf(f"b_raw{k}", [P, TIME // B_FOLD]) for k in range(BODY)]
        xt_hi = [sbuf(f"xt_hi{u}", [P, UNIT], F32R) for u in range(UNITS)]
        xt_lo = [sbuf(f"xt_lo{u}", [P, UNIT], F32R) for u in range(UNITS)]
        a_hl = [sbuf(f"a_hl{i}", [P, STRIDE, 2, 2, HL], F32R) for i in range(2)]
        at = [sbuf(f"at{i}", [P, TIME], F32R) for i in range(2)]
        bt = [sbuf(f"bt{i}", [P, UNITS * CHUNKS, HL], F32R) for i in range(2)]
        m_sel = [sbuf(f"m_sel{i}", [P, P]) for i in range(2)]
        y_t = sbuf("y_t", [P, P])
        y_rows = [sbuf(f"y_rows{i}", [P, P]) for i in range(2)]
        g = [sbuf(f"g{i}", [P, P], F32R) for i in range(2)]

        t_bank = [psum(f"t_bank{i}") for i in range(2)]
        f_bank = [psum(f"f_bank{i}") for i in range(2)]
        y_bank = [psum(f"y_bank{i}") for i in range(2)]
        a_bank = psum("a_bank")
        small = psum("small")
        e_ps = small[:, 0:RANK]
        g_ps = small[:, P:2 * P]
        b_ps = small[:, 2 * P:4 * P]

        ids_in = sem("ids_in")
        w_in = sem("w_in")
        x_loaded = [sem(f"x_loaded{k}") for k in range(BODY)]
        a_loaded = [sem(f"a_loaded{k}") for k in range(BODY)]
        b_loaded = [sem(f"b_loaded{k}") for k in range(BODY)]
        stored = [sem(f"stored{k}") for k in range(BODY)]
        zeroed = sem("zeroed")
        ident_made = sem("ident_made")
        consts_made = sem("consts_made")
        t_done = sem("t_done")
        hi_done = sem("hi_done")
        lo_done = sem("lo_done")
        y_done = sem("y_done")
        f_done = sem("f_done")
        evacuated = sem("evacuated")
        m_picked = sem("m_picked")
        y_copied = sem("y_copied")
        e_done = sem("e_done")
        rows_copied = sem("rows_copied")
        g_done = sem("g_done")
        g_rounded = sem("g_rounded")
        g_split = sem("g_split")
        a_rounded = sem("a_rounded")
        a_split = sem("a_split")
        b_turned = sem("b_turned")
        b_rounded = sem("b_rounded")
        b_split = sem("b_split")
        a_turned = sem("a_turned")
        at_copied = sem("at_copied")

        block = ctx.enter_context(nc.Block())

        @block.sync
        def _(sp):
            def load_x(q, k):
                sp.dma_start(x_in[k][:], x[BODY * q + k]).then_inc(x_loaded[k], 16)

            def load_a(q, k, adapter):
                sp.dma_start(a_raw[k][:].rearrange("p j r -> p (j r)"),
                             a_dram[adapter]).then_inc(a_loaded[k], 16)

            def load_b(q, k, adapter):
                sp.dma_start(b_raw[k][:], b_dram[adapter]).then_inc(b_loaded[k], 16)

            def adapter_of(batch):
                return sp.value_load(ids[0:1, 1, bass.ds(batch, 1)], min_val=0,
                                     max_val=lora_a.shape[0] - 1)

            sp.dma_start(ids[0:1, 0, :], cond_ids).then_inc(ids_in, 16)
            sp.dma_start(ids[0:1, 1, :], adapter_ids).then_inc(ids_in, 16)
            load_x(0, 0)
            sp.wait_ge(ids_in, 32)
            for k in range(BODY):
                adapter = adapter_of(k)
                load_b(0, k, adapter)
                load_a(0, k, adapter)
                if k == 0:
                    sp.dma_start(m_all[:], weights.rearrange("m c d -> c m d")).then_inc(w_in, 16)
                if 0 < k < BODY - 1:
                    load_x(0, k)

            def turn(q, last):
                for k in range(BODY):
                    b = BODY * q + k
                    if not last:
                        adapter = adapter_of(b + BODY)
                        sp.wait_ge(a_split, b + 1)
                        load_a(q + 1, k, adapter)
                        sp.wait_ge(b_turned, b + 1)
                        load_b(q + 1, k, adapter)
                    if not last or k == 0:
                        if live(UNITS * b):
                            sp.wait_ge(f_done, UNITS * b)
                        if k == 0:
                            load_x(q, BODY - 1)
                        else:
                            load_x(q + 1, k - 1)
                    if live(b):
                        sp.wait_ge(evacuated, UNITS * b)
                        sp.dma_start(out[b - 1], x_out[(k - 1) % BODY][:]).then_inc(stored[(k - 1) % BODY], 16)

            turn(0, False)
            with sp.Fori(1, TURNS - 1) as q:
                turn(q, False)
            turn(TURNS - 1, True)
            sp.wait_ge(evacuated, UNITS * BATCHES)
            sp.dma_start(out[BATCHES - 1], x_out[BODY - 1][:]).then_inc(stored[BODY - 1], 16)
            for k in range(BODY):
                sp.wait_ge(stored[k], 16 * TURNS)

        @block.gpsimd
        def _(pool):
            nc.gpsimd.memset(ident[:], 0.0).then_inc(zeroed, 1)
            pool.wait_ge(zeroed, 1)
            nc.gpsimd.affine_select(out=ident[:], in_=ident[:], compare_op=ALU.not_equal, fill=1.0, base=0,
                                    pattern=[[-1, P]], channel_multiplier=1).then_inc(ident_made, 1)

            def split_a(k, b):
                part = a_hl[k // 2 % 2][:, :, k % 2, :, :]
                hi, lo = part[:, :, :, 0:RANK], part[:, :, :, RANK:HL]
                both = a_raw[k][:].rearrange("p j (o r) -> p j o r", o=1).to_broadcast([P, STRIDE, 2, RANK])
                nc.gpsimd.tensor_copy(hi, both).then_inc(a_rounded, 1)
                pool.wait_ge(a_rounded, b + 1)
                nc.gpsimd.tensor_tensor(lo, both, hi, ALU.subtract).then_inc(a_split, 1)

            pool.wait_ge(ids_in, 32)
            for k in range(BODY - 1):
                pool.wait_ge(a_loaded[k], 16)
                split_a(k, k)
            pool.wait_ge(consts_made, 1)

            def turn(q, last):
                for k in range(BODY):
                    b = BODY * q + k
                    if live(UNITS * (b - 1)):
                        pool.wait_ge(f_done, UNITS * (b - 1))
                    ka, qa = (k + 3) % BODY, q + (k + 3) // BODY
                    if not last or k == 0:
                        pool.wait_ge(a_loaded[ka], 16 * (qa + 1))
                        done = 2 * b + 2 if k % 2 else 2 * b
                        if live(done):
                            pool.wait_ge(a_turned, done)
                    cond = pool.value_load(ids[0:1, 0, bass.ds(b, 1)], min_val=0, max_val=CONDITIONS - 1)
                    nc.gpsimd.tensor_copy(m_sel[k % 2][:], m_all[:, cond, :]).then_inc(m_picked, 1)
                    if not last or k == 0:
                        split_a(ka, b + 3)

            turn(0, False)
            with pool.Fori(1, TURNS - 1) as q:
                turn(q, False)
            turn(TURNS - 1, True)

        @block.scalar
        def _(act):
            def round_unit(s, u):
                i = (u + AHEAD) % UNITS
                act.wait_ge(t_done, s + AHEAD + 1)
                if live(s + AHEAD + 1 - UNITS):
                    act.wait_ge(y_done, s + AHEAD + 1 - UNITS)
                nc.scalar.copy(xt_hi[i][:], t_bank[u % 2][:]).then_inc(hi_done, 1)

            def evacuate(k, u, count):
                act.wait_ge(f_done, count)
                nc.scalar.copy(x_out[k][:, UNIT * u:UNIT * (u + 1)], f_bank[u % 2][:]).then_inc(evacuated, 1)

            round_unit(-2, UNITS - 2)
            round_unit(-1, UNITS - 1)

            def turn(q, first, last):
                for k in range(BODY):
                    for u in range(UNITS):
                        s = SLOTS * q + UNITS * k + u
                        f = (UNITS * k + u - BEHIND - 1) % SLOTS
                        if not (first and UNITS * k + u < BEHIND + 1):
                            if f % UNITS == 0:
                                used = q if UNITS * k + u >= BEHIND + 1 else q - 1
                                if live(used):
                                    act.wait_ge(stored[f // UNITS], 16 * used)
                            evacuate(f // UNITS, f % UNITS, s - BEHIND)
                        if not (last and UNITS * k + u + AHEAD >= SLOTS):
                            round_unit(s, u)

            turn(0, True, False)
            with act.Fori(1, TURNS - 1) as q:
                turn(q, False, False)
            turn(TURNS - 1, False, True)
            for n in range(UNITS * BATCHES - BEHIND - 1, UNITS * BATCHES):
                if n % UNITS == 0:
                    act.wait_ge(stored[BODY - 1], 16 * (TURNS - 1))
                evacuate(n % SLOTS // UNITS, n % UNITS, n + 1)

        @block.vector
        def _(dve):
            def rest_of_unit(s, u):
                i = (u + AHEAD) % UNITS
                dve.wait_ge(hi_done, s + AHEAD + 1)
                nc.vector.tensor_tensor(xt_lo[i][:], t_bank[u % 2][:], xt_hi[i][:], ALU.subtract).then_inc(lo_done, 1)

            def split_b(k, b):
                part = bt[k % 2][:].rearrange("p (h f) c -> p h f c", h=B_FOLD)
                hi, lo = part[:, :, :, 0:RANK], part[:, :, :, RANK:HL]
                turned = b_ps.rearrange("p (f r h) -> p h f r", f=2, h=B_FOLD)
                dve.wait_ge(b_turned, b + 1)
                if live(UNITS * (b - 1)):
                    dve.wait_ge(y_done, UNITS * (b - 1))
                nc.vector.tensor_copy(hi, turned).then_inc(b_rounded, 1)
                dve.wait_ge(b_rounded, b + 1)
                nc.vector.tensor_tensor(lo, turned, hi, ALU.subtract).then_inc(b_split, 1)

            def copy_at(pair, part, count, used_units):
                dve.wait_ge(a_turned, count)
                if live(used_units):
                    dve.wait_ge(f_done, used_units)
                to = at[pair % 2][:].rearrange("m (p j) -> m p j", j=STRIDE)
                nc.vector.tensor_copy(to[:, :, A_CHUNKS * part:A_CHUNKS * (part + 1)],
                                      a_bank[:].rearrange("m (j p) -> m p j", p=P)).then_inc(at_copied, 1)

            def low_rank(k, b):
                i = (k - 1) % 2
                dve.wait_ge(y_done, UNITS * b)
                nc.vector.tensor_copy(y_t[0:HL, :], y_bank[i][0:HL, 0:P]).then_inc(y_copied, 1)
                dve.wait_ge(e_done, b)
                nc.vector.tensor_copy(y_rows[i][:, 4 * RANK * i:4 * RANK * (i + 1)].rearrange("c (n r) -> c n r", r=RANK),
                                      e_ps.rearrange("c (n r) -> c n r", n=1).to_broadcast([P, 4, RANK])).then_inc(rows_copied, 1)
                dve.wait_ge(g_done, b)
                if live(UNITS * (b - 2)):
                    dve.wait_ge(f_done, UNITS * (b - 2))
                nc.vector.tensor_copy(g[i][:], g_ps).then_inc(g_rounded, 1)
                dve.wait_ge(g_rounded, b)
                lo = slice(4 * RANK * i + HL, 4 * RANK * (i + 1))
                nc.vector.tensor_tensor(g[i][lo, :], g_ps[lo, :], g[i][lo, :], ALU.subtract).then_inc(g_split, 1)

            dve.wait_ge(ident_made, 1)
            nc.vector.tensor_copy(ident_r[:], ident[:]).then_inc(zeroed, 1)
            nc.vector.tensor_tensor(halves_sum[:], ident[:, 0:RANK], ident[:, RANK:HL], ALU.add).then_inc(zeroed, 1)
            nc.vector.memset(y_t[:], 0.0).then_inc(zeroed, 1)
            nc.vector.memset(y_rows[0][:], 0.0).then_inc(zeroed, 1)
            nc.vector.memset(y_rows[1][:], 0.0).then_inc(zeroed, 1)
            rest_of_unit(-2, UNITS - 2)
            split_b(0, 0)
            rest_of_unit(-1, UNITS - 1)
            dve.wait_ge(w_in, 16)
            nc.vector.tensor_tensor(m_all[:], m_all[:],
                                    ident[:].rearrange("p (m d) -> p m d", m=1).to_broadcast([P, CONDITIONS, P]),
                                    ALU.add).then_inc(consts_made, 1)
            copy_at(0, 0, 1, 0)
            copy_at(0, 1, 2, 0)
            dve.wait_ge(zeroed, 6)

            def turn(q, first, last):
                for k in range(BODY):
                    b = BODY * q + k
                    for u in range(UNITS):
                        s = SLOTS * q + UNITS * k + u
                        if u == 0 and not (first and k == 0):
                            low_rank(k, b)
                        if not (last and UNITS * k + u + AHEAD >= SLOTS):
                            rest_of_unit(s, u)
                        if u == 1 and not (last and k == BODY - 1):
                            split_b((k + 1) % BODY, b + 1)
                        if u in (0, 2) and not (last and k == BODY - 1):
                            part = u // 2 + (0 if k % 2 else 2)
                            pair = ((k + 1) // 2)
                            start = b + 1 if k % 2 else b
                            copy_at(pair, part, 2 * b + 2 + u // 2 + 1, UNITS * (start - 2))

            turn(0, True, False)
            with dve.Fori(1, TURNS - 1) as q:
                turn(q, False, False)
            turn(TURNS - 1, False, True)
            low_rank(0, BATCHES)

        @block.tensor
        def _(pe):
            def transpose_unit(s, position, turn_of_x):
                k, u = position // UNITS % BODY, position % UNITS
                if u == 0:
                    pe.wait_ge(x_loaded[k], 16 * (turn_of_x + 1))
                if live(s + AHEAD - 1):
                    pe.wait_ge(lo_done, s + AHEAD - 1)
                for c in range(CHUNKS):
                    col = UNIT * u + P * c
                    last = nc.tensor.transpose(t_bank[u % 2][:, P * c:P * (c + 1)], x_in[k][:, col:col + P], ident[:])
                last.then_inc(t_done, 1)

            def y_unit(k, u, s, b):
                pe.wait_ge(lo_done, s + 1)
                if u == 0:
                    pe.wait_ge(b_split, b + 1)
                for c in range(CHUNKS):
                    for half in (xt_hi, xt_lo):
                        last = nc.tensor.matmul(y_bank[k % 2][0:HL, 0:P], bt[k % 2][:, CHUNKS * u + c, :],
                                                half[u][:, P * c:P * (c + 1)],
                                                start=(u == 0 and c == 0 and half is xt_hi),
                                                stop=(u == UNITS - 1 and c == CHUNKS - 1 and half is xt_lo))
                last.then_inc(y_done, 1)

            def sum_halves(k, b):
                pe.wait_ge(y_copied, b)
                nc.tensor.matmul(e_ps, y_t[:], halves_sum[:], start=True, stop=True).then_inc(e_done, 1)

            def mix_low_rank(k, b):
                pe.wait_ge(rows_copied, b)
                nc.tensor.matmul(g_ps, y_rows[(k - 1) % 2][:], m_sel[(k - 1) % 2][:],
                                 start=True, stop=True).then_inc(g_done, 1)

            def mix_unit(k, u, s, b):
                if live(s - BEHIND - 1):
                    pe.wait_ge(evacuated, s - BEHIND - 1)
                if u == 0:
                    pe.wait_ge(m_picked, b)
                nc.tensor.matmul(f_bank[u % 2][:], m_sel[(k - 1) % 2][:],
                                 x_in[(k - 1) % BODY][:, UNIT * u:UNIT * (u + 1)], start=True, stop=False)

            def add_low_rank(k, u, b):
                if u == 0:
                    pe.wait_ge(g_split, b)
                    if k % 2:
                        pe.wait_ge(at_copied, 2 * b + 2)
                nc.tensor.matmul(f_bank[u % 2][:], g[(k - 1) % 2][:],
                                 at[(k - 1) % BODY // 2][:, UNIT * u:UNIT * (u + 1)],
                                 start=False, stop=True).then_inc(f_done, 1)

            def turn_b(k, b):
                for f in range(2):
                    last = nc.tensor.transpose(b_ps[:, P * f:P * (f + 1)], b_raw[k][:, P * f:P * (f + 1)], ident[:])
                last.then_inc(b_turned, 1)

            def turn_a(pair, part, before):
                if live(before):
                    pe.wait_ge(at_copied, before)
                for c in range(A_CHUNKS):
                    j = A_CHUNKS * part + c
                    rows = a_hl[pair % 2][:, j].rearrange("p b d c -> p (b d c)")
                    last = nc.tensor.matmul(a_bank[:, P * c:P * (c + 1)], rows, ident_r[:], start=True, stop=True)
                last.then_inc(a_turned, 1)

            pe.wait_ge(ident_made, 1)
            transpose_unit(-2, 0, 0)
            transpose_unit(-1, 1, 0)
            pe.wait_ge(b_loaded[0], 16)
            turn_b(0, 0)
            pe.wait_ge(zeroed, 6)
            pe.wait_ge(a_split, 2)
            turn_a(0, 0, 0)
            turn_a(0, 1, 1)

            def turn(q, first, last):
                for k in range(BODY):
                    b = BODY * q + k
                    for u in range(UNITS):
                        s = SLOTS * q + UNITS * k + u
                        position = UNITS * k + u + AHEAD
                        behind = not (first and k == 0)
                        if not (last and position >= SLOTS):
                            transpose_unit(s, position, q + position // SLOTS)
                        if u == 0 and behind:
                            sum_halves(k, b)
                        if behind:
                            mix_unit(k, u, s, b)
                        if u == 0 and behind:
                            mix_low_rank(k, b)
                        y_unit(k, u, s, b)
                        if u == 1 and not (last and k == BODY - 1):
                            kb, qb = (k + 1) % BODY, q + (k + 1) // BODY
                            pe.wait_ge(b_loaded[kb], 16 * (qb + 1))
                            turn_b(kb, b + 1)
                        if u in (0, 2) and not (last and k == BODY - 1):
                            if k % 2 and u == 0:
                                pe.wait_ge(a_split, b + 3)
                            turn_a((k + 1) // 2, u // 2 + (0 if k % 2 else 2), 2 * b + 2 + u // 2)
                        if behind:
                            add_low_rank(k, u, b)

            turn(0, True, False)
            with pe.Fori(1, TURNS - 1) as q:
                turn(q, False, False)
            turn(TURNS - 1, False, True)
            for u in range(UNITS):
                if u == 0:
                    sum_halves(0, BATCHES)
                mix_unit(0, u, UNITS * BATCHES + u, BATCHES)
                if u == 0:
                    mix_low_rank(0, BATCHES)
                add_low_rank(0, u, BATCHES)


_INS = ['x', 'itok_B_0_15', 'itok_B_4_50', 'L0_cond_weights', 'L1_cond_A', 'L1_cond_B']


def kernel(**inputs):
    import numpy as np
    import concourse.bacc as bacc
    from concourse.bass_utils import run_bass_kernel_spmd

    nc = bacc.Bacc("TRN2", target_bir_lowering=False, num_devices=1)
    arrays, args = {}, []
    for name in _INS:
        a = np.ascontiguousarray(inputs[name])
        if name.startswith("itok"):
            a = a.reshape(1, -1)
        arrays[f"in_{name}"] = a
        args.append(nc.dram_tensor(f"in_{name}", a.shape, mybir.dt.from_np(a.dtype), kind="ExternalInput").ap())
    out = nc.dram_tensor("out", (BATCHES, CHANNELS, TIME), F32, kind="ExternalOutput").ap()
    cond_lora_residual(nc, *args, out)
    result = run_bass_kernel_spmd(nc, [arrays], core_ids=[0])
    return result.results[0]["out"]
```

```python
from contextlib import ExitStack

import concourse.bass as bass
from concourse import mybir

F32 = mybir.dt.float32
F32R = mybir.dt.float32r
I32 = mybir.dt.int32
ALU = mybir.AluOpType
AX = mybir.AxisListType

P = 128
BATCHES, CHANNELS, TIME = 64, 128, 2048
CONDITIONS = 16
RANK = 16
HL = 2 * RANK
UNIT = 512
UNITS = TIME // UNIT
CHUNKS = UNIT // P
BLOCK = 32
STRIDE = TIME // BLOCK
BODY = 4
TURNS = BATCHES // BODY
SLOTS = BODY * UNITS
AHEAD = 2
BEHIND = UNITS
B_FOLD = TIME // 256
A_PARTS = 4
A_BLOCKS = STRIDE // A_PARTS


def live(count):
    return not (isinstance(count, int) and count <= 0)


def cond_lora_residual(nc, x, cond_ids, adapter_ids, weights, lora_a, lora_b, out):
    a_dram = lora_a.rearrange("n (p j) r -> n p (j r)", j=STRIDE)
    b_dram = lora_b.rearrange("n r (h f) -> n (r h) f", h=B_FOLD)

    with ExitStack() as ctx:
        def sbuf(name, shape, dtype=F32):
            return ctx.enter_context(nc.sbuf_tensor(name, shape, dtype))

        def psum(name):
            return ctx.enter_context(nc.psum_tensor(name, [P, UNIT], F32))

        def sem(name):
            return ctx.enter_context(nc.semaphore(name))

        ident = sbuf("ident", [P, P])
        m_all = sbuf("m_all", [P, CONDITIONS, P])
        ids = sbuf("ids", [1, 2, BATCHES], I32)

        x_in = [sbuf(f"x_in{k}", [P, TIME]) for k in range(BODY)]
        x_out = [sbuf(f"x_out{k}", [P, TIME]) for k in range(BODY)]
        a_raw = [sbuf(f"a_raw{i}", [P, STRIDE, RANK]) for i in range(2)]
        b_raw = [sbuf(f"b_raw{k}", [P, TIME // B_FOLD]) for k in range(BODY)]
        xt_hi = [sbuf(f"xt_hi{u}", [P, UNIT], F32R) for u in range(UNITS)]
        xt_lo = [sbuf(f"xt_lo{u}", [P, UNIT], F32R) for u in range(UNITS)]
        a_hl = [sbuf(f"a_hl{i}", [P, STRIDE, HL], F32R) for i in range(2)]
        at_part = [sbuf(f"at_part{i}", [P, A_BLOCKS, BLOCK]) for i in range(2)]
        at = [sbuf(f"at{i}", [P, TIME], F32R) for i in range(2)]
        bt = [sbuf(f"bt{i}", [P, UNITS * CHUNKS, HL], F32R) for i in range(2)]
        m_sel = [sbuf(f"m_sel{i}", [P, P]) for i in range(2)]
        y_t = sbuf("y_t", [P, P])
        y_rows = [sbuf(f"y_rows{i}", [P, P]) for i in range(2)]
        g = [sbuf(f"g{i}", [P, P], F32R) for i in range(2)]

        t_bank = [psum(f"t_bank{i}") for i in range(2)]
        f_bank = [psum(f"f_bank{i}") for i in range(2)]
        y_bank = [psum(f"y_bank{i}") for i in range(2)]
        small = psum("small")
        e_ps = small[:, 0:P]
        g_ps = small[:, P:2 * P]
        b_ps = psum("b_bank")[:, 0:2 * P]

        ids_in = sem("ids_in")
        w_in = sem("w_in")
        x0_loaded = [sem(f"x0_loaded{u}") for u in range(UNITS)]
        x_loaded = [sem(f"x_loaded{k}") for k in range(BODY)]
        a_loaded = [sem(f"a_loaded{i}") for i in range(2)]
        b_loaded = [sem(f"b_loaded{k}") for k in range(BODY)]
        stored = [sem(f"stored{k}") for k in range(BODY)]
        ident_zeroed = sem("ident_zeroed")
        zeroed = sem("zeroed")
        ident_made = sem("ident_made")
        consts_made = sem("consts_made")
        t_done = sem("t_done")
        hi_done = sem("hi_done")
        lo_done = sem("lo_done")
        y_done = sem("y_done")
        f_done = sem("f_done")
        evacuated = sem("evacuated")
        m_picked = sem("m_picked")
        y_copied = sem("y_copied")
        e_done = sem("e_done")
        rows_copied = sem("rows_copied")
        g_done = sem("g_done")
        g_rounded = sem("g_rounded")
        g_split = sem("g_split")
        a_rounded = sem("a_rounded")
        a_split = sem("a_split")
        b_turned = sem("b_turned")
        b_rounded = sem("b_rounded")
        b_split = sem("b_split")
        a_turned = sem("a_turned")
        at_made = sem("at_made")

        block = ctx.enter_context(nc.Block())

        @block.sync
        def _(sp):
            def load_x(q, k):
                sp.dma_start(x_in[k][:], x[BODY * q + k]).then_inc(x_loaded[k], 16)

            def load_a(k, adapter):
                for copy in range(2):
                    at_partition = 2 * BLOCK * (k % 2) + BLOCK * copy
                    sp.dma_start(a_raw[k // 2][at_partition:at_partition + BLOCK].rearrange("p j r -> p (j r)"),
                                 a_dram[adapter]).then_inc(a_loaded[k // 2], 16)

            def load_b(k, adapter):
                sp.dma_start(b_raw[k][:], b_dram[adapter]).then_inc(b_loaded[k], 16)

            def adapter_of(batch):
                return sp.value_load(ids[0:1, 1, bass.ds(batch, 1)], min_val=0,
                                     max_val=lora_a.shape[0] - 1)

            sp.dma_start(ids[0:1, 0, :], cond_ids).then_inc(ids_in, 16)
            sp.dma_start(ids[0:1, 1, :], adapter_ids).then_inc(ids_in, 16)
            for u in range(UNITS):
                sp.dma_start(x_in[0][:, UNIT * u:UNIT * (u + 1)],
                             x[0, :, UNIT * u:UNIT * (u + 1)]).then_inc(x0_loaded[u], 16)
                if u == 1:
                    sp.wait_ge(ids_in, 32)
                    adapter = adapter_of(0)
                    load_b(0, adapter)
            load_x(0, 1)
            load_a(0, adapter)
            adapter = adapter_of(1)
            load_b(1, adapter)
            load_a(1, adapter)
            sp.dma_start(m_all[:], weights.rearrange("m c d -> c m d")).then_inc(w_in, 16)
            load_x(0, 2)
            for k in (2, 3):
                adapter = adapter_of(k)
                load_b(k, adapter)
                load_a(k, adapter)

            def turn(q, last):
                for k in range(BODY):
                    b = BODY * q + k
                    if not last:
                        adapter = adapter_of(b + BODY)
                        sp.wait_ge(a_split, b + 1 if k % 2 else b + 2)
                        load_a(k, adapter)
                        sp.wait_ge(b_turned, b + 1)
                        load_b(k, adapter)
                    if not last or k == 0:
                        if live(UNITS * b):
                            sp.wait_ge(f_done, UNITS * b)
                        if k == 0:
                            load_x(q, BODY - 1)
                        else:
                            load_x(q + 1, k - 1)
                    if live(b):
                        sp.wait_ge(evacuated, UNITS * b)
                        sp.dma_start(out[b - 1], x_out[(k - 1) % BODY][:]).then_inc(stored[(k - 1) % BODY], 16)

            turn(0, False)
            with sp.Fori(1, TURNS - 1) as q:
                turn(q, False)
            turn(TURNS - 1, True)
            for u in range(UNITS):
                sp.wait_ge(evacuated, UNITS * (BATCHES - 1) + u + 1)
                sp.dma_start(out[BATCHES - 1, :, UNIT * u:UNIT * (u + 1)],
                             x_out[BODY - 1][:, UNIT * u:UNIT * (u + 1)]).then_inc(stored[BODY - 1], 16)
            for k in range(BODY):
                sp.wait_ge(stored[k], 16 * (TURNS if k < BODY - 1 else TURNS - 1 + UNITS))

        @block.gpsimd
        def _(pool):
            nc.gpsimd.memset(ident[:], 0.0).then_inc(ident_zeroed, 1)
            pool.wait_ge(ident_zeroed, 1)
            nc.gpsimd.affine_select(out=ident[:], in_=ident[:], compare_op=ALU.not_equal, fill=1.0, base=0,
                                    pattern=[[-1, P]], channel_multiplier=1).then_inc(ident_made, 1)

            def split_a(k, n):
                js = slice(STRIDE // 2 * (k % 2), STRIDE // 2 * (k % 2 + 1))
                raw, part = a_raw[k // 2][:, js, :], a_hl[k // 2][:, js, :]
                nc.gpsimd.tensor_copy(part[:, :, 0:RANK], raw).then_inc(a_rounded, 1)
                pool.wait_ge(a_rounded, n + 1)
                nc.gpsimd.tensor_tensor(part[:, :, RANK:HL], raw, part[:, :, 0:RANK], ALU.subtract).then_inc(a_split, 1)

            pool.wait_ge(a_loaded[0], 64)
            split_a(0, 0)
            split_a(1, 1)
            pool.wait_ge(ids_in, 32)
            pool.wait_ge(consts_made, 1)

            def turn(q, last):
                for k in range(BODY):
                    b = BODY * q + k
                    if live(UNITS * (b - 1)):
                        pool.wait_ge(f_done, UNITS * (b - 1))
                    ka, qa = (k + 2) % BODY, q + (k + 2) // BODY
                    more = not last or k < BODY - 2
                    if more and k % 2 == 0:
                        pool.wait_ge(a_loaded[ka // 2], 64 * (qa + 1))
                        if live(2 * b):
                            pool.wait_ge(a_turned, 2 * b)
                    cond = pool.value_load(ids[0:1, 0, bass.ds(b, 1)], min_val=0, max_val=CONDITIONS - 1)
                    nc.gpsimd.tensor_copy(m_sel[k % 2][:], m_all[:, cond, :]).then_inc(m_picked, 1)
                    if more:
                        split_a(ka, b + 2)

            turn(0, False)
            with pool.Fori(1, TURNS - 1) as q:
                turn(q, False)
            turn(TURNS - 1, True)

        @block.scalar
        def _(act):
            def round_unit(s, u):
                i = (u + AHEAD) % UNITS
                act.wait_ge(t_done, s + AHEAD + 1)
                if live(s + AHEAD + 1 - UNITS):
                    act.wait_ge(y_done, s + AHEAD + 1 - UNITS)
                nc.scalar.copy(xt_hi[i][:], t_bank[u % 2][:]).then_inc(hi_done, 1)

            def evacuate(k, u, count):
                act.wait_ge(f_done, count)
                nc.scalar.copy(x_out[k][:, UNIT * u:UNIT * (u + 1)], f_bank[u % 2][:]).then_inc(evacuated, 1)

            def place_at(k, part):
                first = A_BLOCKS * (2 * (k % 2) + part)
                to = at[k // 2][:].rearrange("m (p j) -> m j p", j=STRIDE)[:, first:first + A_BLOCKS, :]
                nc.scalar.copy(to, at_part[part][:]).then_inc(at_made, 1)

            round_unit(-2, UNITS - 2)
            round_unit(-1, UNITS - 1)
            for part in range(2):
                act.wait_ge(a_turned, part + 1)
                place_at(0, part)

            def turn(q, first, last):
                for k in range(BODY):
                    b = BODY * q + k
                    for u in range(UNITS):
                        s = SLOTS * q + UNITS * k + u
                        f = (UNITS * k + u - BEHIND - 1) % SLOTS
                        if not (first and UNITS * k + u < BEHIND + 1):
                            if f % UNITS == 0:
                                used = q if UNITS * k + u >= BEHIND + 1 else q - 1
                                if live(used):
                                    act.wait_ge(stored[f // UNITS], 16 * used)
                            evacuate(f // UNITS, f % UNITS, s - BEHIND)
                        if not (last and UNITS * k + u + AHEAD >= SLOTS):
                            round_unit(s, u)
                        if u in (2, 3) and not (last and k == BODY - 1):
                            act.wait_ge(a_turned, 2 * b + 1 + u)
                            if u == 2 and k % 2 and live(UNITS * (b - 1)):
                                act.wait_ge(f_done, UNITS * (b - 1))
                            place_at((k + 1) % BODY, u - 2)

            turn(0, True, False)
            with act.Fori(1, TURNS - 1) as q:
                turn(q, False, False)
            turn(TURNS - 1, False, True)
            for n in range(UNITS * BATCHES - BEHIND - 1, UNITS * BATCHES):
                if n % UNITS == 0:
                    act.wait_ge(stored[BODY - 1], 16 * (TURNS - 1))
                evacuate(n % SLOTS // UNITS, n % UNITS, n + 1)

        @block.vector
        def _(dve):
            def rest_of_unit(s, u):
                i = (u + AHEAD) % UNITS
                dve.wait_ge(hi_done, s + AHEAD + 1)
                nc.vector.tensor_tensor(xt_lo[i][:], t_bank[u % 2][:], xt_hi[i][:], ALU.subtract).then_inc(lo_done, 1)

            def split_b(k, b):
                part = bt[k % 2][:].rearrange("p (h f) c -> p h f c", h=B_FOLD)
                hi, lo = part[:, :, :, 0:RANK], part[:, :, :, RANK:HL]
                turned = b_ps.rearrange("p (f r h) -> p h f r", f=2, h=B_FOLD)
                dve.wait_ge(b_turned, b + 1)
                if live(UNITS * (b - 1)):
                    dve.wait_ge(y_done, UNITS * (b - 1))
                nc.vector.tensor_copy(hi, turned).then_inc(b_rounded, 1)
                dve.wait_ge(b_rounded, b + 1)
                nc.vector.tensor_tensor(lo, turned, hi, ALU.subtract).then_inc(b_split, 1)

            def turn_a(k, part):
                first = A_BLOCKS * (2 * (k % 2) + part)
                nc.vector.transpose(at_part[part][:], a_hl[k // 2][:, first:first + A_BLOCKS, :].bitcast(F32)).then_inc(a_turned, 1)

            def low_rank(k, b):
                i = (k - 1) % 2
                dve.wait_ge(y_done, UNITS * b)
                nc.vector.tensor_copy(y_t[0:HL, :], y_bank[i][0:HL, 0:P]).then_inc(y_copied, 1)
                dve.wait_ge(e_done, b)
                halves = e_ps[:, 0:HL].rearrange("c (n h r) -> c n r h", n=1, h=2).to_broadcast([P, 4, RANK, 2])
                rows = y_rows[i][:, 4 * RANK * i:4 * RANK * (i + 1)].rearrange("c (n r) -> c n r", r=RANK)
                nc.vector.tensor_reduce(rows, halves, AX.X, ALU.add).then_inc(rows_copied, 1)
                dve.wait_ge(g_done, b)
                if live(UNITS * (b - 2)):
                    dve.wait_ge(f_done, UNITS * (b - 2))
                nc.vector.tensor_copy(g[i][:], g_ps).then_inc(g_rounded, 1)
                dve.wait_ge(g_rounded, b)
                lo = slice(4 * RANK * i + HL, 4 * RANK * (i + 1))
                nc.vector.tensor_tensor(g[i][lo, :], g_ps[lo, :], g[i][lo, :], ALU.subtract).then_inc(g_split, 1)

            dve.wait_ge(ident_made, 1)
            nc.vector.memset(y_t[:], 0.0).then_inc(zeroed, 1)
            nc.vector.memset(y_rows[0][:], 0.0).then_inc(zeroed, 1)
            nc.vector.memset(y_rows[1][:], 0.0).then_inc(zeroed, 1)
            rest_of_unit(-2, UNITS - 2)
            split_b(0, 0)
            rest_of_unit(-1, UNITS - 1)
            dve.wait_ge(w_in, 16)
            nc.vector.tensor_tensor(m_all[:], m_all[:],
                                    ident[:].rearrange("p (m d) -> p m d", m=1).to_broadcast([P, CONDITIONS, P]),
                                    ALU.add).then_inc(consts_made, 1)
            dve.wait_ge(a_split, 1)
            turn_a(0, 0)
            turn_a(0, 1)
            dve.wait_ge(zeroed, 3)

            def turn(q, first, last):
                for k in range(BODY):
                    b = BODY * q + k
                    for u in range(UNITS):
                        s = SLOTS * q + UNITS * k + u
                        if u == 0 and not (first and k == 0):
                            low_rank(k, b)
                        if not (last and UNITS * k + u + AHEAD >= SLOTS):
                            rest_of_unit(s, u)
                        if u == 0 and not (last and k == BODY - 1):
                            split_b((k + 1) % BODY, b + 1)
                        if u in (1, 2) and not (last and k == BODY - 1):
                            if u == 1:
                                dve.wait_ge(a_split, b + 2)
                            if live(2 * b + u):
                                dve.wait_ge(at_made, 2 * b + u)
                            turn_a((k + 1) % BODY, u - 1)

            turn(0, True, False)
            with dve.Fori(1, TURNS - 1) as q:
                turn(q, False, False)
            turn(TURNS - 1, False, True)
            low_rank(0, BATCHES)

        @block.tensor
        def _(pe):
            def transpose_unit(s, position, turn_of_x):
                k, u = position // UNITS % BODY, position % UNITS
                loads = turn_of_x + 1 - (k == 0)
                if not live(loads):
                    pe.wait_ge(x0_loaded[u], 16)
                elif u == 0:
                    pe.wait_ge(x_loaded[k], 16 * loads)
                if live(s + AHEAD - 1):
                    pe.wait_ge(lo_done, s + AHEAD - 1)
                for c in range(CHUNKS):
                    col = UNIT * u + P * c
                    last = nc.tensor.transpose(t_bank[u % 2][:, P * c:P * (c + 1)], x_in[k][:, col:col + P], ident[:])
                last.then_inc(t_done, 1)

            def y_unit(k, u, s, b):
                pe.wait_ge(lo_done, s + 1)
                if u == 0:
                    pe.wait_ge(b_split, b + 1)
                for c in range(CHUNKS):
                    for half in (xt_hi, xt_lo):
                        last = nc.tensor.matmul(y_bank[k % 2][0:HL, 0:P], bt[k % 2][:, CHUNKS * u + c, :],
                                                half[u][:, P * c:P * (c + 1)],
                                                start=(u == 0 and c == 0 and half is xt_hi),
                                                stop=(u == UNITS - 1 and c == CHUNKS - 1 and half is xt_lo))
                last.then_inc(y_done, 1)

            def sum_halves(k, b):
                pe.wait_ge(y_copied, b)
                nc.tensor.transpose(e_ps, y_t[:], ident[:]).then_inc(e_done, 1)

            def mix_low_rank(k, b):
                pe.wait_ge(rows_copied, b)
                nc.tensor.matmul(g_ps, y_rows[(k - 1) % 2][:], m_sel[(k - 1) % 2][:],
                                 start=True, stop=True).then_inc(g_done, 1)

            def mix_unit(k, u, s, b):
                if live(s - BEHIND - 1):
                    pe.wait_ge(evacuated, s - BEHIND - 1)
                if u == 0:
                    pe.wait_ge(m_picked, b)
                nc.tensor.matmul(f_bank[u % 2][:], m_sel[(k - 1) % 2][:],
                                 x_in[(k - 1) % BODY][:, UNIT * u:UNIT * (u + 1)], start=True, stop=False)

            def add_low_rank(k, u, b):
                if u == 0:
                    pe.wait_ge(g_split, b)
                    if k % 2:
                        pe.wait_ge(at_made, 2 * b + 2)
                nc.tensor.matmul(f_bank[u % 2][:], g[(k - 1) % 2][:],
                                 at[(k - 1) % BODY // 2][:, UNIT * u:UNIT * (u + 1)],
                                 start=False, stop=True).then_inc(f_done, 1)

            def turn_b(k, b):
                for f in range(2):
                    last = nc.tensor.transpose(b_ps[:, P * f:P * (f + 1)], b_raw[k][:, P * f:P * (f + 1)], ident[:])
                last.then_inc(b_turned, 1)

            pe.wait_ge(ident_made, 1)
            transpose_unit(-2, 0, 0)
            transpose_unit(-1, 1, 0)
            pe.wait_ge(b_loaded[0], 16)
            turn_b(0, 0)
            pe.wait_ge(zeroed, 3)

            def turn(q, first, last):
                for k in range(BODY):
                    b = BODY * q + k
                    for u in range(UNITS):
                        s = SLOTS * q + UNITS * k + u
                        position = UNITS * k + u + AHEAD
                        behind = not (first and k == 0)
                        if not (last and position >= SLOTS):
                            transpose_unit(s, position, q + position // SLOTS)
                        if u == 0 and behind:
                            sum_halves(k, b)
                        if behind:
                            mix_unit(k, u, s, b)
                        if u == 0 and behind:
                            mix_low_rank(k, b)
                        if u > 0 and behind:
                            add_low_rank(k, u, b)
                        y_unit(k, u, s, b)
                        if u == 0 and not (last and k == BODY - 1):
                            kb, qb = (k + 1) % BODY, q + (k + 1) // BODY
                            pe.wait_ge(b_loaded[kb], 16 * (qb + 1))
                            turn_b(kb, b + 1)
                        if u == 0 and behind:
                            add_low_rank(k, u, b)

            turn(0, True, False)
            with pe.Fori(1, TURNS - 1) as q:
                turn(q, False, False)
            turn(TURNS - 1, False, True)
            for u in range(UNITS):
                if u == 0:
                    sum_halves(0, BATCHES)
                mix_unit(0, u, UNITS * BATCHES + u, BATCHES)
                if u == 0:
                    mix_low_rank(0, BATCHES)
                add_low_rank(0, u, BATCHES)


_INS = ['x', 'itok_B_0_15', 'itok_B_4_50', 'L0_cond_weights', 'L1_cond_A', 'L1_cond_B']


def kernel(**inputs):
    import numpy as np
    import concourse.bacc as bacc
    from concourse.bass_utils import run_bass_kernel_spmd

    nc = bacc.Bacc("TRN2", target_bir_lowering=False, num_devices=1)
    arrays, args = {}, []
    for name in _INS:
        a = np.ascontiguousarray(inputs[name])
        if name.startswith("itok"):
            a = a.reshape(1, -1)
        arrays[f"in_{name}"] = a
        args.append(nc.dram_tensor(f"in_{name}", a.shape, mybir.dt.from_np(a.dtype), kind="ExternalInput").ap())
    out = nc.dram_tensor("out", (BATCHES, CHANNELS, TIME), F32, kind="ExternalOutput").ap()
    cond_lora_residual(nc, *args, out)
    result = run_bass_kernel_spmd(nc, [arrays], core_ids=[0])
    return result.results[0]["out"]
```

```python
from contextlib import ExitStack

import concourse.bass as bass
from concourse import mybir

F32 = mybir.dt.float32
F32R = mybir.dt.float32r
I32 = mybir.dt.int32
ALU = mybir.AluOpType
AX = mybir.AxisListType

P = 128
BATCHES, CHANNELS, TIME = 64, 128, 2048
CONDITIONS = 16
RANK = 16
HL = 2 * RANK
UNIT = 512
UNITS = TIME // UNIT
CHUNKS = UNIT // P
STEP = 2
SPAN = STEP * P
SPANS = TIME // SPAN
BLOCK = 32
STRIDE = TIME // BLOCK
BODY = 4
TURNS = BATCHES // BODY
SLOTS = BODY * UNITS
AHEAD = 2
BEHIND = UNITS
LAG = 2
BY_UNITS = 3
A_PARTS = 4
A_BLOCKS = STRIDE // A_PARTS


def live(count):
    return not (isinstance(count, int) and count <= 0)


def cond_lora_residual(nc, x, cond_ids, adapter_ids, weights, lora_a, lora_b, out):
    a_dram = lora_a.rearrange("n (p j) r -> n p (j r)", j=STRIDE)
    b_dram = lora_b.rearrange("n r (v g j) -> n g r v j", v=SPANS, g=P // BLOCK)

    with ExitStack() as ctx:
        def sbuf(name, shape, dtype=F32):
            return ctx.enter_context(nc.sbuf_tensor(name, shape, dtype))

        def psum(name):
            return ctx.enter_context(nc.psum_tensor(name, [P, UNIT], F32))

        def sem(name):
            return ctx.enter_context(nc.semaphore(name))

        ident = sbuf("ident", [P, P])
        w_all = sbuf("w_all", [P, CONDITIONS, P])
        ids = sbuf("ids", [1, 2, BATCHES], I32)

        x_in = [sbuf(f"x_in{k}", [P, TIME]) for k in range(BODY)]
        x_out = [sbuf(f"x_out{k}", [P, TIME]) for k in range(BODY)]
        a_raw = [sbuf(f"a_raw{i}", [P, STRIDE, RANK]) for i in range(2)]
        b_raw = [sbuf(f"b_raw{i}", [P, SPANS, STEP * BLOCK]) for i in range(2)]
        xt = [sbuf(f"xt{u}", [P, CHUNKS, 2, P], F32R) for u in range(UNITS)]
        a_hl = [sbuf(f"a_hl{i}", [P, STRIDE, HL], F32R) for i in range(2)]
        at_part = [sbuf(f"at_part{i}", [P, A_BLOCKS, BLOCK]) for i in range(2)]
        at = [sbuf(f"at{i}", [P, TIME], F32R) for i in range(2)]
        b_pair = sbuf("b_pair", [P, UNITS * CHUNKS, BLOCK])
        bt = [sbuf(f"bt{i}", [P, UNITS * CHUNKS, HL], F32R) for i in range(2)]
        w_first = [sbuf(f"w_first{k}", [P, P]) for k in range(2)]
        m_sel = [sbuf(f"m_sel{k}", [P, P]) for k in range(BODY)]
        y_t = sbuf("y_t", [P, P])
        y_rows = [sbuf(f"y_rows{i}", [P, P]) for i in range(2)]
        g = [sbuf(f"g{i}", [P, P], F32R) for i in range(2)]

        t_bank = [psum(f"t_bank{i}") for i in range(2)]
        f_bank = [psum(f"f_bank{u}") for u in range(UNITS)]
        y_bank = [psum(f"y_bank{i}") for i in range(2)]
        y_ps = [y_bank[i][0:HL, 0:2 * P] for i in range(2)]
        e_ps = [y_bank[i][:, 2 * P:3 * P] for i in range(2)]
        g_ps = [y_bank[i][:, 3 * P:4 * P] for i in range(2)]

        ids_in = sem("ids_in")
        w_in = sem("w_in")
        w_first_in = [sem(f"w_first_in{k}") for k in range(2)]
        first_loaded = [sem(f"first_loaded{n}") for n in range(BY_UNITS * UNITS)]
        x_loaded = [sem(f"x_loaded{k}") for k in range(BODY)]
        a_loaded = [sem(f"a_loaded{i}") for i in range(2)]
        b_loaded = [sem(f"b_loaded{i}") for i in range(2)]
        stored = [sem(f"stored{k}") for k in range(BODY)]
        ident_zeroed = sem("ident_zeroed")
        zeroed = sem("zeroed")
        ident_made = sem("ident_made")
        t_done = sem("t_done")
        hi_done = sem("hi_done")
        lo_done = sem("lo_done")
        y_done = sem("y_done")
        f_done = sem("f_done")
        evacuated = sem("evacuated")
        first_a_rounded = sem("first_a_rounded")
        first_a_split = sem("first_a_split")
        a_rounded = sem("a_rounded")
        a_split = sem("a_split")
        m_picked = sem("m_picked")
        y_joined = sem("y_joined")
        e_done = sem("e_done")
        rows_made = sem("rows_made")
        g_done = sem("g_done")
        g_rounded = sem("g_rounded")
        g_split = sem("g_split")
        first_b_rounded = sem("first_b_rounded")
        first_b_split = sem("first_b_split")
        b_rounded = sem("b_rounded")
        b_split = sem("b_split")
        b_turned = sem("b_turned")
        a_turned = sem("a_turned")
        at_made = sem("at_made")

        def a_half(k):
            js = slice(STRIDE // 2 * (k % 2), STRIDE // 2 * (k % 2 + 1))
            return a_raw[k // 2][:, js, :], a_hl[k // 2][:, js, 0:RANK], a_hl[k // 2][:, js, RANK:HL]

        block = ctx.enter_context(nc.Block())

        @block.sync
        def _(sp):
            def load_x(q, k):
                sp.dma_start(x_in[k][:], x[BODY * q + k]).then_inc(x_loaded[k], 16)

            def load_a(k, adapter):
                for copy in range(2):
                    at_partition = 2 * BLOCK * (k % 2) + BLOCK * copy
                    sp.dma_start(a_raw[k // 2][at_partition:at_partition + BLOCK].rearrange("p j r -> p (j r)"),
                                 a_dram[adapter]).then_inc(a_loaded[k // 2], 16)

            def load_b(k, adapter):
                sp.dma_start(b_raw[k // 2][k % 2::2], b_dram[adapter]).then_inc(b_loaded[k // 2], 16)

            def adapter_of(batch):
                return sp.value_load(ids[0:1, 1, bass.ds(batch, 1)], min_val=0,
                                     max_val=lora_a.shape[0] - 1)

            def load_first(n):
                b, cols = n // UNITS, slice(n % UNITS * UNIT, (n % UNITS + 1) * UNIT)
                sp.dma_start(x_in[b][:, cols], x[b, :, cols]).then_inc(first_loaded[n], 16)

            sp.dma_start(ids[0:1, 0, :], cond_ids).then_inc(ids_in, 16)
            sp.dma_start(ids[0:1, 1, :], adapter_ids).then_inc(ids_in, 16)
            for n in range(UNITS):
                load_first(n)
            sp.wait_ge(ids_in, 32)
            adapters = [adapter_of(0), adapter_of(1)]
            load_b(0, adapters[0])
            load_b(1, adapters[1])
            for k in range(2):
                cond = sp.value_load(ids[0:1, 0, k:k + 1], min_val=0, max_val=CONDITIONS - 1)
                sp.dma_start(w_first[k][:], weights[cond]).then_inc(w_first_in[k], 16)
            load_first(4)
            load_first(5)
            load_a(0, adapters[0])
            load_a(1, adapters[1])
            load_first(6)
            load_first(7)
            load_first(8)
            adapters = [adapter_of(2), adapter_of(3)]
            load_a(2, adapters[0])
            load_a(3, adapters[1])
            load_b(2, adapters[0])
            load_b(3, adapters[1])
            for n in range(9, BY_UNITS * UNITS):
                load_first(n)
            sp.dma_start(w_all[:], weights.rearrange("m c d -> c m d")).then_inc(w_in, 16)

            def turn(q, last):
                for k in range(BODY):
                    b = BODY * q + k
                    if not last:
                        adapter = adapter_of(b + BODY)
                        if not live(b):
                            sp.wait_ge(first_a_split, 2)
                        elif k % 2 == 0:
                            sp.wait_ge(a_split, b)
                        load_a(k, adapter)
                        sp.wait_ge(b_turned, BODY // 2 * q + k // 2 + 1)
                        load_b(k, adapter)
                    if not last or k == 0:
                        if live(UNITS * b):
                            sp.wait_ge(f_done, UNITS * b)
                        if k == 0:
                            load_x(q, BODY - 1)
                        else:
                            load_x(q + 1, k - 1)
                    if live(b) and not (last and k == BODY - 1):
                        sp.wait_ge(evacuated, UNITS * b)
                        sp.dma_start(out[b - 1], x_out[(k - 1) % BODY][:]).then_inc(stored[(k - 1) % BODY], 16)

            turn(0, False)
            with sp.Fori(1, TURNS - 1) as q:
                turn(q, False)
            turn(TURNS - 1, True)
            for n in range(UNITS * (BATCHES - 2), UNITS * BATCHES):
                b, cols = n // UNITS, slice(n % UNITS * UNIT, (n % UNITS + 1) * UNIT)
                sp.wait_ge(evacuated, n + 1)
                sp.dma_start(out[b, :, cols], x_out[b % BODY][:, cols]).then_inc(stored[b % BODY], 16)
            for k in range(BODY):
                sp.wait_ge(stored[k], 16 * (TURNS if k < BODY - 2 else TURNS - 1 + UNITS))

        @block.gpsimd
        def _(pool):
            nc.gpsimd.memset(ident[:], 0.0).then_inc(ident_zeroed, 1)
            pool.wait_ge(ident_zeroed, 1)
            nc.gpsimd.affine_select(out=ident[:], in_=ident[:], compare_op=ALU.not_equal, fill=1.0, base=0,
                                    pattern=[[-1, P]], channel_multiplier=1).then_inc(ident_made, 1)

            def split_a(k, n):
                raw, hi, lo = a_half(k)
                nc.gpsimd.tensor_copy(hi, raw).then_inc(a_rounded, 1)
                pool.wait_ge(a_rounded, n - 1)
                nc.gpsimd.tensor_tensor(lo, raw, hi, ALU.subtract).then_inc(a_split, 1)

            def split_b(k, b):
                turned = b_pair[:, :, k % 2::2]
                hi, lo = bt[k % 2][:, :, 0:RANK], bt[k % 2][:, :, RANK:HL]
                nc.gpsimd.tensor_copy(hi, turned).then_inc(b_rounded, 1)
                pool.wait_ge(b_rounded, b - 1)
                nc.gpsimd.tensor_tensor(lo, turned, hi, ALU.subtract).then_inc(b_split, 1)

            def pick_m(k, b):
                cond = pool.value_load(ids[0:1, 0, bass.ds(b, 1)], min_val=0, max_val=CONDITIONS - 1)
                nc.gpsimd.tensor_tensor(m_sel[k][:], w_all[:, cond, :], ident[:], ALU.add).then_inc(m_picked, 1)

            pool.wait_ge(ids_in, 32)
            pool.wait_ge(ident_made, 1)
            for k in range(2):
                pool.wait_ge(w_first_in[k], 16)
                nc.gpsimd.tensor_tensor(m_sel[k][:], w_first[k][:], ident[:], ALU.add).then_inc(m_picked, 1)
            pool.wait_ge(first_a_rounded, 2)
            raw, hi, lo = a_half(1)
            nc.gpsimd.tensor_tensor(lo, raw, hi, ALU.subtract).then_inc(first_a_split, 1)
            pool.wait_ge(a_loaded[1], 64)
            split_a(2, 2)
            pool.wait_ge(w_in, 16)

            def turn(q, first, last):
                for k in range(1 if first else 0, BODY):
                    b = BODY * q + k
                    splits = not last or k < BODY - 2
                    ka, qa = (k + 2) % BODY, q + (k + 2) // BODY
                    if splits and k % 2 == 0:
                        pool.wait_ge(a_turned, 2 * b)
                        pool.wait_ge(a_loaded[ka // 2], 64 * (qa + 1))
                    if not last or k < BODY - 1:
                        if live(UNITS * (b - 2)):
                            pool.wait_ge(f_done, UNITS * (b - 2))
                        pool.wait_ge(y_done, UNITS * b)
                        pool.wait_ge(b_turned, BODY // 2 * q + (k + 1) // 2 + 1)
                        pick_m((k + 1) % BODY, b + 1)
                        split_b((k + 1) % BODY, b + 1)
                    if splits:
                        split_a(ka, b + 2)

            turn(0, True, False)
            with pool.Fori(1, TURNS - 1) as q:
                turn(q, False, False)
            turn(TURNS - 1, False, True)

        @block.scalar
        def _(act):
            def round_unit(s, u):
                i = (u + AHEAD) % UNITS
                act.wait_ge(t_done, s + AHEAD + 1)
                if live(s + AHEAD + 1 - UNITS):
                    act.wait_ge(y_done, s + AHEAD + 1 - UNITS)
                turned = t_bank[u % 2][:].rearrange("p (n c) -> p n c", n=CHUNKS)
                nc.scalar.copy(xt[i][:, :, 0, :], turned).then_inc(hi_done, 1)

            def evacuate(k, u, count):
                act.wait_ge(f_done, count)
                nc.scalar.copy(x_out[k][:, UNIT * u:UNIT * (u + 1)], f_bank[u][:]).then_inc(evacuated, 1)

            def place_at(k, part):
                first = A_BLOCKS * (2 * (k % 2) + part)
                to = at[k // 2][:].rearrange("m (p j) -> m j p", j=STRIDE)[:, first:first + A_BLOCKS, :]
                nc.scalar.copy(to, at_part[part][:]).then_inc(at_made, 1)

            for s in range(-AHEAD, UNITS - 1):
                round_unit(s, s % UNITS)
            act.wait_ge(a_loaded[0], 64)
            for h in range(2):
                raw, hi, _ = a_half(h)
                nc.scalar.copy(hi, raw).then_inc(first_a_rounded, 1)
            round_unit(UNITS - 1, UNITS - 1)

            def turn(q, first, last):
                for k in range(1 if first else 0, BODY):
                    b = BODY * q + k
                    for u in range(UNITS):
                        s = SLOTS * q + UNITS * k + u
                        if not (last and UNITS * k + u + AHEAD >= SLOTS):
                            round_unit(s, u)
                        f = (UNITS * k + u - BEHIND - LAG) % SLOTS
                        if not (first and UNITS * k + u < BEHIND + LAG):
                            if f % UNITS == 0:
                                used = q if UNITS * k + u >= BEHIND + LAG else q - 1
                                if live(used):
                                    act.wait_ge(stored[f // UNITS], 16 * used)
                            evacuate(f // UNITS, f % UNITS, s - BEHIND - LAG + 1)
                        if first and k == 1 and u < 2:
                            for part in range(2):
                                act.wait_ge(a_turned, 2 * u + part + 1)
                                place_at(u, part)
                        if u == 0 and not (first and k == 1):
                            act.wait_ge(a_turned, 2 * b + 2)
                            place_at(k, 1)
                        if u == 3 and not (last and k == BODY - 1):
                            act.wait_ge(a_turned, 2 * b + 3)
                            if k % 2 and live(UNITS * (b - 1)):
                                act.wait_ge(f_done, UNITS * (b - 1))
                            place_at((k + 1) % BODY, 0)

            turn(0, True, False)
            with act.Fori(1, TURNS - 1) as q:
                turn(q, False, False)
            turn(TURNS - 1, False, True)
            for n in range(UNITS * BATCHES - BEHIND - LAG, UNITS * BATCHES):
                if n % UNITS == 0:
                    act.wait_ge(stored[BODY - 1], 16 * (TURNS - 1))
                evacuate(n % SLOTS // UNITS, n % UNITS, n + 1)

        @block.vector
        def _(dve):
            def rest_of_unit(s, u):
                i = (u + AHEAD) % UNITS
                dve.wait_ge(hi_done, s + AHEAD + 1)
                turned = t_bank[u % 2][:].rearrange("p (n c) -> p n c", n=CHUNKS)
                nc.vector.tensor_tensor(xt[i][:, :, 1, :], turned, xt[i][:, :, 0, :], ALU.subtract).then_inc(lo_done, 1)

            def turn_b(i):
                chunks = b_raw[i][:].rearrange("p v (i c) -> p v c i", c=STEP)
                nc.vector.transpose(b_pair[:].rearrange("p (v c) i -> p v c i", c=STEP), chunks).then_inc(b_turned, 1)

            def turn_a(k, part):
                first = A_BLOCKS * (2 * (k % 2) + part)
                nc.vector.transpose(at_part[part][:], a_hl[k // 2][:, first:first + A_BLOCKS, :].bitcast(F32)).then_inc(a_turned, 1)

            def join_y(k, b):
                dve.wait_ge(y_done, UNITS * b)
                halves = y_ps[(k - 1) % 2].rearrange("r (h c) -> r c h", h=2)
                nc.vector.tensor_reduce(y_t[0:HL, :], halves, AX.X, ALU.add).then_inc(y_joined, 1)

            def make_rows(k, b):
                i = (k - 1) % 2
                dve.wait_ge(e_done, b)
                halves = e_ps[i][:, 0:HL].rearrange("c (n h r) -> c n r h", n=1, h=2).to_broadcast([P, 4, RANK, 2])
                rows = y_rows[i][:, 4 * RANK * i:4 * RANK * (i + 1)].rearrange("c (n r) -> c n r", r=RANK)
                nc.vector.tensor_reduce(rows, halves, AX.X, ALU.add).then_inc(rows_made, 1)

            def make_g(k, b):
                i = (k - 1) % 2
                dve.wait_ge(g_done, b)
                if live(UNITS * (b - 2)):
                    dve.wait_ge(f_done, UNITS * (b - 2))
                nc.vector.tensor_copy(g[i][:], g_ps[i]).then_inc(g_rounded, 1)
                dve.wait_ge(g_rounded, b)
                lo = slice(4 * RANK * i + HL, 4 * RANK * (i + 1))
                nc.vector.tensor_tensor(g[i][lo, :], g_ps[i][lo, :], g[i][lo, :], ALU.subtract).then_inc(g_split, 1)

            dve.wait_ge(ident_made, 1)
            nc.vector.memset(y_t[:], 0.0).then_inc(zeroed, 1)
            nc.vector.memset(y_rows[0][:], 0.0).then_inc(zeroed, 1)
            nc.vector.memset(y_rows[1][:], 0.0).then_inc(zeroed, 1)
            rest_of_unit(-2, UNITS - 2)
            dve.wait_ge(b_loaded[0], 2 * 16)
            turn_b(0)
            dve.wait_ge(b_turned, 1)
            for k in range(2):
                turned = b_pair[:, :, k::2]
                nc.vector.tensor_copy(bt[k][:, :, 0:RANK], turned).then_inc(first_b_rounded, 1)
                dve.wait_ge(first_b_rounded, k + 1)
                nc.vector.tensor_tensor(bt[k][:, :, RANK:HL], turned, bt[k][:, :, 0:RANK],
                                        ALU.subtract).then_inc(first_b_split, 1)
                if k == 0:
                    rest_of_unit(-1, UNITS - 1)
                rest_of_unit(k, k)
            rest_of_unit(AHEAD, AHEAD)
            dve.wait_ge(first_a_rounded, 1)
            raw, hi, lo = a_half(0)
            nc.vector.tensor_tensor(lo, raw, hi, ALU.subtract).then_inc(first_a_split, 1)
            rest_of_unit(UNITS - 1, UNITS - 1)
            dve.wait_ge(first_a_split, 2)
            dve.wait_ge(first_b_split, 2)
            dve.wait_ge(zeroed, 3)

            def turn(q, first, last):
                for k in range(1 if first else 0, BODY):
                    b = BODY * q + k
                    for u in range(UNITS):
                        s = SLOTS * q + UNITS * k + u
                        if u == 0:
                            join_y(k, b)
                            if first and k == 1:
                                turn_a(0, 0)
                            make_rows(k, b)
                        if u == 1:
                            make_g(k, b)
                        if first and k == 1 and u == 1:
                            for part in range(2):
                                dve.wait_ge(at_made, part + 1)
                                turn_a(1, part)
                        if not (last and UNITS * k + u + AHEAD >= SLOTS):
                            rest_of_unit(s, u)
                        if first and k == 1 and u == 0:
                            turn_a(0, 1)
                        if u >= 2 and not (last and k == BODY - 1):
                            if u == 2:
                                dve.wait_ge(a_split, b)
                            dve.wait_ge(at_made, 2 * b + u - 1)
                            turn_a((k + 1) % BODY, u - 2)
                        if k % 2 and u == (2 if first and k == 1 else 0) and not (last and k == BODY - 1):
                            i, qi = (k + 1) // 2 % 2, q + (k + 1) // BODY
                            dve.wait_ge(b_loaded[i], 2 * 16 * (qi + 1))
                            if live(b - 1):
                                dve.wait_ge(b_split, b - 1)
                            turn_b(i)

            turn(0, True, False)
            with dve.Fori(1, TURNS - 1) as q:
                turn(q, False, False)
            turn(TURNS - 1, False, True)
            join_y(0, BATCHES)
            make_rows(0, BATCHES)
            make_g(0, BATCHES)

        @block.tensor
        def _(pe):
            def transpose_unit(s, position, turn_of_x):
                k, u = position // UNITS % BODY, position % UNITS
                loads = turn_of_x + 1 - (k < BY_UNITS)
                if not live(loads):
                    pe.wait_ge(first_loaded[UNITS * k + u], 16)
                elif u == 0:
                    pe.wait_ge(x_loaded[k], 16 * loads)
                if live(s + AHEAD - 1):
                    pe.wait_ge(lo_done, s + AHEAD - 1)
                for c in range(CHUNKS):
                    first = UNIT * u + SPAN * (c // STEP) + c % STEP
                    columns = x_in[k][:, first:first + SPAN - 1:STEP]
                    last = nc.tensor.transpose(t_bank[u % 2][:, P * c:P * (c + 1)], columns, ident[:])
                last.then_inc(t_done, 1)

            def y_unit(k, u, s, b):
                pe.wait_ge(lo_done, s + 1)
                if u == 0:
                    if isinstance(b, int) and b < 2:
                        pe.wait_ge(first_b_split, b + 1)
                    else:
                        pe.wait_ge(b_split, b - 1)
                for c in range(CHUNKS):
                    last = nc.tensor.matmul(y_ps[k % 2], bt[k % 2][:, CHUNKS * u + c, :],
                                            xt[u][:, c, :, :].rearrange("t hl c -> t (hl c)"),
                                            start=(u == 0 and c == 0), stop=(u == UNITS - 1 and c == CHUNKS - 1))
                last.then_inc(y_done, 1)

            def sum_halves(k, b):
                pe.wait_ge(y_joined, b)
                nc.tensor.transpose(e_ps[(k - 1) % 2], y_t[:], ident[:]).then_inc(e_done, 1)

            def mix_low_rank(k, b):
                pe.wait_ge(rows_made, b)
                nc.tensor.matmul(g_ps[(k - 1) % 2], y_rows[(k - 1) % 2][:], m_sel[(k - 1) % BODY][:],
                                 start=True, stop=True).then_inc(g_done, 1)

            def mix_unit(k, u, b):
                if u == 0:
                    pe.wait_ge(m_picked, b)
                nc.tensor.matmul(f_bank[u][:], m_sel[(k - 1) % BODY][:],
                                 x_in[(k - 1) % BODY][:, UNIT * u:UNIT * (u + 1)], start=True, stop=False)

            def add_low_rank(k, u, b):
                if u == 0:
                    pe.wait_ge(g_split, b)
                    if k % 2:
                        pe.wait_ge(at_made, 2 * b + 2)
                nc.tensor.matmul(f_bank[u][:], g[(k - 1) % 2][:],
                                 at[(k - 1) % BODY // 2][:, UNIT * u:UNIT * (u + 1)],
                                 start=False, stop=True).then_inc(f_done, 1)

            pe.wait_ge(ident_made, 1)
            transpose_unit(-2, 0, 0)
            transpose_unit(-1, 1, 0)
            for u in range(UNITS):
                transpose_unit(u, u + AHEAD, 0)
                y_unit(0, u, u, 0)
            pe.wait_ge(zeroed, 3)

            def turn(q, first, last):
                for k in range(1 if first else 0, BODY):
                    b = BODY * q + k
                    for u in range(UNITS):
                        s = SLOTS * q + UNITS * k + u
                        position = UNITS * k + u + AHEAD
                        if not (last and position >= SLOTS):
                            transpose_unit(s, position, q + position // SLOTS)
                        if u == 2:
                            add_low_rank(k, 0, b)
                            add_low_rank(k, 1, b)
                        if live(s - BEHIND - UNITS + 1):
                            pe.wait_ge(evacuated, s - BEHIND - UNITS + 1)
                        if u == 1:
                            mix_low_rank(k, b)
                        mix_unit(k, u, b)
                        if u == 0:
                            sum_halves(k, b)
                        if u >= 2:
                            add_low_rank(k, u, b)
                        y_unit(k, u, s, b)

            turn(0, True, False)
            with pe.Fori(1, TURNS - 1) as q:
                turn(q, False, False)
            turn(TURNS - 1, False, True)
            for u in range(UNITS):
                pe.wait_ge(evacuated, UNITS * (BATCHES - 2) + u + 1)
                mix_unit(0, u, BATCHES)
                if u == 0:
                    sum_halves(0, BATCHES)
                if u == 1:
                    mix_low_rank(0, BATCHES)
                for ready in {2: (0, 1, 2), 3: (3,)}.get(u, ()):
                    add_low_rank(0, ready, BATCHES)


_INS = ['x', 'itok_B_0_15', 'itok_B_4_50', 'L0_cond_weights', 'L1_cond_A', 'L1_cond_B']


def kernel(**inputs):
    import numpy as np
    import concourse.bacc as bacc
    from concourse.bass_utils import run_bass_kernel_spmd

    nc = bacc.Bacc("TRN2", target_bir_lowering=False, num_devices=1)
    arrays, args = {}, []
    for name in _INS:
        a = np.ascontiguousarray(inputs[name])
        if name.startswith("itok"):
            a = a.reshape(1, -1)
        arrays[f"in_{name}"] = a
        args.append(nc.dram_tensor(f"in_{name}", a.shape, mybir.dt.from_np(a.dtype), kind="ExternalInput").ap())
    out = nc.dram_tensor("out", (BATCHES, CHANNELS, TIME), F32, kind="ExternalOutput").ap()
    cond_lora_residual(nc, *args, out)
    result = run_bass_kernel_spmd(nc, [arrays], core_ids=[0])
    return result.results[0]["out"]
```
